# Optimizing a Trainium2 kernel written in Bass

```python
import numpy as np
import jax
import jax.numpy as jnp

def _softmax(x, axis=-1):
    return jax.nn.softmax(x, axis=axis)

def _gelu(x):
    return jax.nn.gelu(x, approximate=True)

def _silu(x):
    return jax.nn.silu(x)

def _sigmoid(x):
    return jax.nn.sigmoid(x)

def _layernorm(x, axis=-1, eps=1e-05):
    m = jnp.mean(x, axis=axis, keepdims=True)
    v = jnp.var(x, axis=axis, keepdims=True)
    return (x - m) / jnp.sqrt(v + eps)

def _scatter_add(tgt, idx, src, axis=0):
    return tgt.at[idx].add(src)

def _segment_sum(src, seg, n):
    return jax.ops.segment_sum(src, seg, n)
kernel_name = 'mk_seq_postln_d1_jaxref_r4_7abe9d'

def setup_inputs(seed: int=0):
    np.random.seed(seed)
    _w = jnp.asarray

    def _L0_attn_setup():
        import math
        import jax, jax.numpy as jnp
        import numpy as np
        B, T, D_MODEL, N_HEADS = (2, 512, 256, 16)
        HEAD_DIM = D_MODEL // N_HEADS

        def _alibi_slopes(n_heads: int) -> np.ndarray:

            def pow2(n):
                start = 2.0 ** (-(8.0 / n))
                return [start * start ** i for i in range(n)]
            if math.log2(n_heads).is_integer():
                s = pow2(n_heads)
            else:
                cp = 2 ** math.floor(math.log2(n_heads))
                base = pow2(cp)
                extra = pow2(2 * cp)[1::2]
                s = base + extra[:n_heads - cp]
            return np.asarray(s, dtype=np.float32)
        SLOPES = jnp.asarray(_alibi_slopes(N_HEADS))
        key = jax.random.key(seed)
        k1, k2, k3 = jax.random.split(key, 3)
        x = jax.random.normal(k1, (B, T, D_MODEL), dtype=jnp.float32)
        Wqkv = jax.random.normal(k2, (D_MODEL, 3 * D_MODEL), dtype=jnp.float32) * 0.02
        Wout = jax.random.normal(k3, (D_MODEL, D_MODEL), dtype=jnp.float32) * 0.02
        return {'x': x, 'Wqkv': Wqkv, 'Wout': Wout}
    _L0_attn_in = _L0_attn_setup()

    def _L0_ffn_setup():
        import jax, jax.numpy as jnp
        import numpy as np
        DIM = 256
        HIDDEN = 768
        SCALE = 1.0 / 127.0

        def _dequant(w_int, dtype):
            return w_int.astype(dtype) * jnp.asarray(SCALE, dtype)
        key = jax.random.key(seed)
        k_x, k_g, k_u, k_d = jax.random.split(key, 4)
        x = jax.random.normal(k_x, (4, 512, DIM), dtype=jnp.float32)
        w_gate = jax.random.randint(k_g, (HIDDEN, DIM), -127, 128, dtype=jnp.int32)
        w_up = jax.random.randint(k_u, (HIDDEN, DIM), -127, 128, dtype=jnp.int32)
        w_down = jax.random.randint(k_d, (DIM, HIDDEN), -127, 128, dtype=jnp.int32)
        return {'x': x, 'w_gate': w_gate, 'w_up': w_up, 'w_down': w_down}
    _L0_ffn_in = _L0_ffn_setup()
    _d = {'L0_attn_x': _L0_attn_in['x'], 'L0_attn_Wqkv': _L0_attn_in['Wqkv'], 'L0_attn_Wout': _L0_attn_in['Wout'], 'L0_ffn_w_gate': _L0_ffn_in['w_gate'], 'L0_ffn_w_up': _L0_ffn_in['w_up'], 'L0_ffn_w_down': _L0_ffn_in['w_down']}
    _x0 = _d['L0_attn_x']
    _d['L0_attn_x'] = jax.random.normal(jax.random.fold_in(jax.random.key(seed), 1), (32, 512, 256), dtype=_x0.dtype)
    del _x0
    return _d

def reference(L0_attn_x, L0_attn_Wqkv, L0_attn_Wout, L0_ffn_w_gate, L0_ffn_w_up, L0_ffn_w_down):

    def _L0_attn_ref(x, Wqkv, Wout):
        import math
        import jax, jax.numpy as jnp
        import numpy as np
        B, T, D_MODEL, N_HEADS = (2, 512, 256, 16)
        HEAD_DIM = D_MODEL // N_HEADS

        def _alibi_slopes(n_heads: int) -> np.ndarray:

            def pow2(n):
                start = 2.0 ** (-(8.0 / n))
                return [start * start ** i for i in range(n)]
            if math.log2(n_heads).is_integer():
                s = pow2(n_heads)
            else:
                cp = 2 ** math.floor(math.log2(n_heads))
                base = pow2(cp)
                extra = pow2(2 * cp)[1::2]
                s = base + extra[:n_heads - cp]
            return np.asarray(s, dtype=np.float32)
        SLOPES = jnp.asarray(_alibi_slopes(N_HEADS))
        Bc, Tc, Dc = x.shape
        qkv = x @ Wqkv
        q, k, v = jnp.split(qkv, 3, axis=-1)
        q = q.reshape(Bc, Tc, N_HEADS, HEAD_DIM)
        k = k.reshape(Bc, Tc, N_HEADS, HEAD_DIM)
        v = v.reshape(Bc, Tc, N_HEADS, HEAD_DIM)
        scale = 1.0 / math.sqrt(HEAD_DIM)
        logits = jnp.einsum('bihd,bjhd->bhij', q, k) * scale
        pos = jnp.arange(Tc, dtype=jnp.float32)
        rel = pos[None, :] - pos[:, None]
        logits = logits + SLOPES[None, :, None, None] * rel[None, None, :, :]
        causal = pos[:, None] >= pos[None, :]
        logits = jnp.where(causal[None, None, :, :], logits, -jnp.inf)
        attn = jax.nn.softmax(logits, axis=-1)
        out = jnp.einsum('bhij,bjhd->bihd', attn, v).reshape(Bc, Tc, Dc)
        return out @ Wout

    def _L0_ffn_ref(x, w_gate, w_up, w_down):
        import jax, jax.numpy as jnp
        import numpy as np
        DIM = 256
        HIDDEN = 768
        SCALE = 1.0 / 127.0

        def _dequant(w_int, dtype):
            return w_int.astype(dtype) * jnp.asarray(SCALE, dtype)
        wg = _dequant(w_gate, x.dtype)
        wu = _dequant(w_up, x.dtype)
        wd = _dequant(w_down, x.dtype)
        gate = jnp.einsum('bsd,hd->bsh', x, wg)
        up = jnp.einsum('bsd,hd->bsh', x, wu)
        h = jax.nn.silu(gate) * up
        return jnp.einsum('bsh,dh->bsd', h, wd)
    x = L0_attn_x
    x = _layernorm(x + _L0_attn_ref(x, L0_attn_Wqkv, L0_attn_Wout), axis=-1)
    x = _layernorm(x + _L0_ffn_ref(x, L0_ffn_w_gate, L0_ffn_w_up, L0_ffn_w_down), axis=-1)
    return x

_drawn_inputs = setup_inputs


def setup_inputs(seed=0):
    import zlib

    import numpy as np

    out = dict(_drawn_inputs(seed))
    spreads = {}
    factors = {}
    for name, (base, spread) in spreads.items():
        noise = np.random.default_rng([zlib.crc32(name.encode()), seed]).standard_normal(out[name].shape)
        drawn = base * np.exp(spread * noise) if base else spread * noise
        out[name] = jnp.asarray(drawn.astype(out[name].dtype))
    for name, factor in factors.items():
        out[name] = (out[name] * factor).astype(out[name].dtype)
    return out
```

```python
from contextlib import ExitStack

import numpy as np

import concourse.bass as bass
from concourse import mybir

F32 = mybir.dt.float32
F32R = mybir.dt.float32r
BF16 = mybir.dt.bfloat16
I32 = mybir.dt.int32
ALU = mybir.AluOpType
ACT = mybir.ActivationFunctionType
AX = mybir.AxisListType

P = 128
HEADS, HEAD_DIM = 16, 16
UNIT_HEADS = P // HEAD_DIM
GROUP = 4
SPLIT_ROWS = 4 * HEAD_DIM
ALIBI_ROWS = 4
MAX_ROWS = 2
ROWS1 = SPLIT_ROWS + ALIBI_ROWS
ROWS2 = ROWS1 + MAX_ROWS
BANK = 512
MASKED = -3.0e38
EPS = 1e-5
W_SCALE = float(np.float32(1.0 / 127.0))


class Sem:

    def __init__(self, handle):
        self.handle, self.count = handle, 0


class Queue:

    def __init__(self):
        self.steps, self.reached = [], {}

    def wait(self, *marks):
        for sem, value in marks:
            if self.reached.get(sem, 0) < value:
                self.reached[sem] = value
                self.steps.append(lambda e, s=sem.handle, v=value: e.wait_ge(s, v))

    def put(self, instruction, sem=None, by=1):
        if sem is None:
            self.steps.append(instruction)
            return None
        self.steps.append(lambda e, f=instruction, s=sem.handle, n=by: f(e).then_inc(s, n))
        sem.count += by
        return (sem, sem.count)

    def play(self, engine):
        for step in self.steps:
            step(engine)


def alibi_slopes():
    start = 2.0 ** (-(8.0 / HEADS))
    return np.asarray([start * start ** i for i in range(HEADS)], dtype=np.float32)


def constants(tokens, scale):
    slopes = alibi_slopes() / np.float32(scale)
    slope_hi = (slopes.view(np.uint32) & np.uint32(0xFFFFF000)).view(np.float32)
    slope_lo = slopes - slope_hi
    position = np.arange(tokens, dtype=np.float32) - tokens // 2
    ones = np.ones(tokens, np.float32)
    rows = np.zeros((ALIBI_ROWS + MAX_ROWS, 2, HEADS, tokens), np.float32)
    for h in range(HEADS):
        rows[0, 0, h], rows[0, 1, h] = slope_hi[h] * ones, position
        rows[1, 0, h], rows[1, 1, h] = slope_lo[h] * ones, position
        rows[2, 0, h], rows[2, 1, h] = position, -slope_hi[h] * ones
        rows[3, 0, h], rows[3, 1, h] = position, -slope_lo[h] * ones
        rows[4, 1, h] = rows[5, 1, h] = -ones
    identity = np.eye(P, dtype=np.float32)
    mask = np.where(np.arange(P)[None, :] > np.arange(P)[:, None], np.float32(MASKED), np.float32(0))
    return rows, np.stack([identity, mask.astype(np.float32)], 1)


def build(nc, x, w_qkv, w_out, w_gate, w_up, w_down, edge_rows, squares, out):
    batches, tokens, dim = x.shape
    hidden = w_gate.shape[0]
    blocks = tokens // P
    kd = dim // P
    kh = hidden // P
    scale = HEAD_DIM ** -0.5
    units = batches * 2
    half_tokens = tokens // 2
    assert tokens == BANK and HEADS == 2 * UNIT_HEADS and kd == 2 and blocks == 4

    with ExitStack() as ctx:
        def sb(name, shape, dt=F32):
            return ctx.enter_context(nc.sbuf_tensor(name, shape, dt))

        def ps(name, shape, dt=F32):
            return ctx.enter_context(nc.psum_tensor(name, shape, dt))

        def sem(name):
            return Sem(ctx.enter_context(nc.semaphore(name)))

        wqkv_hi, wqkv_lo = sb("wqkv_hi", [P, kd, 3 * dim], F32R), sb("wqkv_lo", [P, kd, 3 * dim], F32R)
        wout_hi, wout_lo = sb("wout_hi", [P, kd, dim], F32R), sb("wout_lo", [P, kd, dim], F32R)
        wgate_t, wup_t = sb("wgate_t", [P, kd, hidden], F32R), sb("wup_t", [P, kd, hidden], F32R)
        wdown_t = sb("wdown_t", [P, kh, dim], F32R)
        ident = sb("ident", [P, P])
        ident_bf, mask_bf = sb("ident_bf", [P, P], BF16), sb("mask_bf", [P, P], BF16)
        minus_half = sb("minus_half", [P, blocks])
        q_rows = [sb(f"q_rows{i}", [P, UNIT_HEADS, tokens], F32R) for i in range(2)]
        k_rows = [sb(f"k_rows{i}", [P, UNIT_HEADS, tokens], F32R) for i in range(2)]
        staged = {n: sb(f"staged_{n}", [P, tokens], F32R) for n in ("q_hi", "q_lo", "k_hi", "k_lo")}
        v_ones = [sb(f"v_ones{i}", [P, blocks, HEADS, 2 * HEAD_DIM]) for i in range(2)]
        x_sb = [sb(f"x_sb{i}", [P, blocks, dim]) for i in range(3)]
        xt_hi, xt_lo = sb("xt_hi", [P, kd, tokens], F32R), sb("xt_lo", [P, kd, tokens], F32R)
        probs = [sb(f"probs{i}", [P, GROUP, tokens]) for i in range(3)]
        row_max = [sb(f"row_max{i}", [P, blocks, UNIT_HEADS]) for i in range(2)]
        max_hi, max_lo = sb("max_hi", [UNIT_HEADS, tokens], F32R), sb("max_lo", [UNIT_HEADS, tokens], F32R)
        pv_t = [sb(f"pv_t{i}", [P, tokens]) for i in range(2)]
        rden = [sb(f"rden{i}", [P, blocks, GROUP]) for i in range(2)]
        attn = sb("attn", [P, blocks, dim])
        x1 = [sb(f"x1_{i}", [P, blocks, dim]) for i in range(2)]
        wide_hi, wide_lo = sb("wide_hi", [P, kd, tokens], F32R), sb("wide_lo", [P, kd, tokens], F32R)
        stats1, moments1 = sb("stats1", [P, blocks, 6]), sb("moments1", [P, blocks, 2])
        stats2, moments2 = sb("stats2", [P, 2, 6]), sb("moments2", [P, 2, 2])
        var1, rstd1 = sb("var1", [P, blocks]), sb("rstd1", [P, blocks])
        var2, rstd2 = sb("var2", [P, 2]), sb("rstd2", [P, 2])
        h_full = [sb(f"h_full{i}", [P, half_tokens]) for i in range(2)]
        h_hi = [sb(f"h_hi{i}", [P, half_tokens], F32R) for i in range(2)]
        h_lo = [sb(f"h_lo{i}", [P, half_tokens], F32R) for i in range(2)]
        result = [sb(f"result{i}", [P, 2, dim]) for i in range(2)]

        bounce = nc.dram_tensor("bounce", [2, 4, HEAD_DIM, UNIT_HEADS, tokens], F32, kind="Internal").ap()

        score_banks = [ps(f"score_bank{i}", [P, BANK]) for i in range(3)]
        work_banks = [ps(f"work_bank{i}", [P, BANK]) for i in range(3)]
        pv_bank = ps("pv_bank", [P, BANK])
        down_bank = ps("down_bank", [P, 2, dim])

        pe, act, dve, pool, sp = Queue(), Queue(), Queue(), Queue(), Queue()

        s_const, s_weights = sem("s_const"), sem("s_weights")
        s_x = [sem(f"s_x{i}") for i in range(3)]
        s_spread = [sem(f"s_spread{i}") for i in range(2)]
        s_bounced = [sem(f"s_bounced{i}") for i in range(2)]
        s_edge = sem("s_edge")
        s_maxrow = [sem(f"s_maxrow{i}") for i in range(2)]
        s_store = [sem(f"s_store{i}") for i in range(2)]
        s_pe_work, s_pe_score, s_pe_pv, s_pe_down = (sem(n) for n in ("s_pe_work", "s_pe_score", "s_pe_pv", "s_pe_down"))
        s_act, s_act_exp, s_dve, s_dve_max, s_pool = (sem(n) for n in ("s_act", "s_act_exp", "s_dve", "s_dve_max", "s_pool"))

        work_free, work_next = [[], [], []], [0]

        def work_bank():
            i = work_next[0] % 3
            work_next[0] += 1
            assert work_free[i] is not None
            pe.wait(*work_free[i])
            work_free[i] = None
            return i, work_banks[i]

        def mm(o, lhs, rhs, start, stop, sem=None, **kw):
            return pe.put(lambda e, o=o, l=lhs, r=rhs: e.matmul(o, l, r, start=start, stop=stop,
                                                                skip_group_check=True, **kw), sem)

        def transpose(o, i, sem=None):
            n = i.shape[0]
            return pe.put(lambda e: e.transpose(o, i, ident[0:n, 0:n]), sem)

        def split_out(i, bank, rows, hi, lo, made, free=(), cols=BANK):
            src = bank[0:rows, 0:cols]
            act.wait(made, *free)
            hi_done = act.put(lambda e: e.activation(hi, src, ACT.Copy), s_act)
            dve.wait(made, hi_done, *free)
            lo_done = dve.put(lambda e: e.tensor_tensor(lo, src, hi.bitcast(F32), ALU.subtract), s_dve)
            work_free[i] = [hi_done, lo_done]
            return hi_done, lo_done

        pending = []

        def defer(f):
            pending.append(f)
            if len(pending) > 1:
                pending.pop(0)()

        def flush():
            while pending:
                pending.pop(0)()

        def flat(buffer, size):
            dims = " ".join("abc"[:len(buffer.shape) - 1])
            return buffer[:].rearrange(f"p {dims} -> p ({dims})")[:, 0:size]

        raw_qkv = flat(probs[0], kd * 3 * dim).rearrange("p (k n) -> p k n", k=kd)
        raw_out = flat(attn, kd * dim).rearrange("p (k n) -> p k n", k=kd)
        gate_f = flat(probs[1], kh * dim).rearrange("p (t n) -> p t n", t=kh)
        up_f = flat(probs[2], kh * dim).rearrange("p (t n) -> p t n", t=kh)
        down_f = flat(v_ones[1], kd * hidden).rearrange("p (t n) -> p t n", t=kd)
        squares_sb = x1[0][:, 0:1, :].rearrange("p a (s n) -> p (a s) n", s=2)

        sp.put(lambda e: e.dma_start(squares_sb, squares), s_const, 16)
        const_in = (s_const, s_const.count)
        sp.put(lambda e: e.dma_start(raw_qkv, w_qkv.rearrange("(k p) n -> p k n", p=P)), s_weights, 16)
        sp.put(lambda e: e.dma_start(raw_out, w_out.rearrange("(k p) n -> p k n", p=P)), s_weights, 16)
        sp.put(lambda e: e.dma_start(gate_f.bitcast(I32), w_gate.rearrange("(t p) n -> p t n", p=P)), s_weights, 16)
        sp.put(lambda e: e.dma_start(up_f.bitcast(I32), w_up.rearrange("(t p) n -> p t n", p=P)), s_weights, 16)
        sp.put(lambda e: e.dma_start(down_f.bitcast(I32), w_down.rearrange("(t p) n -> p t n", p=P)), s_weights, 16)
        weights_in = (s_weights, s_weights.count)

        def load_x(b, *free):
            sp.wait(*free)
            return sp.put(lambda e: e.dma_start(x_sb[b % 3][:, :, :], x[b].rearrange("(t p) d -> p t d", p=P)),
                          s_x[b % 3], 16)

        x_in = {b: load_x(b) for b in range(min(2, batches))}

        dve.wait(const_in)
        dve.put(lambda e: e.tensor_copy(ident[:, :], squares_sb[:, 0, :]), s_dve)
        dve.put(lambda e: e.tensor_copy(ident_bf[:, :], squares_sb[:, 0, :]), s_dve)
        dve.put(lambda e: e.tensor_copy(mask_bf[:, :], squares_sb[:, 1, :]), s_dve)
        dve.put(lambda e: e.memset(minus_half[:, :], -0.5), s_dve)
        ident_done = dve.put(lambda e: e.memset(v_ones[0][:, :, :, HEAD_DIM:], 1.0), s_dve)
        dve.wait(weights_in)
        hi = dve.put(lambda e: e.tensor_copy(wqkv_hi[:, :, :], raw_qkv), s_dve)
        hi2 = dve.put(lambda e: e.tensor_copy(wout_hi[:, :, :], raw_out), s_dve)
        dve.put(lambda e: e.tensor_copy(gate_f, gate_f.bitcast(I32)), s_dve)
        dve.put(lambda e: e.tensor_copy(up_f, up_f.bitcast(I32)), s_dve)
        as_float = dve.put(lambda e: e.tensor_copy(down_f, down_f.bitcast(I32)), s_dve)
        dve.wait(hi, hi2)
        dve.put(lambda e: e.tensor_tensor(wqkv_lo[:, :, :], raw_qkv, wqkv_hi[:, :, :].bitcast(F32), ALU.subtract), s_dve)
        wqkv_done = dve.put(lambda e: e.tensor_tensor(wout_lo[:, :, :], raw_out, wout_hi[:, :, :].bitcast(F32), ALU.subtract), s_dve)
        dve.wait(as_float)
        pe.wait(ident_done, as_float)
        for src, dst, tiles, parts in ((gate_f, wgate_t, kd, kh), (up_f, wup_t, kd, kh), (down_f, wdown_t, kh, kd)):
            for c in range(tiles):
                for r0 in range(0, parts, 4):
                    n = min(4, parts - r0)
                    i, bank = work_bank()
                    for r in range(n):
                        made = transpose(bank[:, r * P:(r + 1) * P], src[:, r0 + r, c * P:(c + 1) * P],
                                         s_pe_work if r == n - 1 else None)
                    act.wait(made)
                    done = act.put(lambda e, d=dst, c=c, r0=r0, n=n, bank=bank:
                                   e.activation(d[:, c, r0 * P:(r0 + n) * P], bank[:, 0:n * P], ACT.Copy), s_act)
                    work_free[i] = [done]
        ffn_weights_done = done
        dve.wait(done)
        v_ones_done = dve.put(lambda e: e.memset(v_ones[1][:, :, :, HEAD_DIM:], 1.0), s_dve)
        n_edge = ALIBI_ROWS + MAX_ROWS
        edge_buf = [probs[i][0:n_edge, 0:2, :] for i in range(2)]
        edge_r = [xt_hi[0:n_edge, :, :], xt_lo[0:n_edge, :, :]]
        last_copy = {}
        turn = 0
        sp.wait(ffn_weights_done, wqkv_done)
        for hf in range(2):
            for side, rows in ((0, q_rows[hf]), (1, k_rows[hf])):
                for h0 in range(0, UNIT_HEADS, 2):
                    z = turn % 2
                    raw = edge_buf[z]
                    if turn >= 2:
                        sp.wait(last_copy[z][0])
                    head = hf * UNIT_HEADS + h0
                    loaded = sp.put(lambda e, raw=raw, side=side, head=head:
                                    e.dma_start(raw, edge_rows[:, side, head:head + 2, :]), s_edge, 16)
                    dve.wait(loaded)
                    if turn >= 2:
                        dve.wait(last_copy[z][1])
                    rounded = dve.put(lambda e, raw=raw, z=z: e.tensor_copy(edge_r[z], raw), s_dve)
                    sp.wait(rounded, ffn_weights_done)
                    n = ALIBI_ROWS if side == 0 else n_edge
                    copied = sp.put(lambda e, rows=rows, n=n, h0=h0, z=z:
                                    e.dma_start(rows[SPLIT_ROWS:SPLIT_ROWS + n, h0:h0 + 2, :].bitcast(F32),
                                                edge_r[z][0:n].bitcast(F32)), s_edge, 16)
                    sp.wait(copied)
                    last_copy[z] = (rounded, copied)
                    turn += 1
        edges_done = copied

        x1_done = {}
        marks = {}

        def got(*keys):
            return [m for k in keys for m in (marks[k] if isinstance(marks[k], list) else [marks[k]])]

        def maybe(*keys):
            return [m for k in keys if k in marks for m in (marks[k] if isinstance(marks[k], list) else [marks[k]])]

        def transposed(src, dst_hi, dst_lo, ready, free, key):
            for c in range(kd):
                i, bank = work_bank()
                pe.wait(*ready)
                for t in range(blocks):
                    made = transpose(bank[:, t * P:(t + 1) * P], src[:, t, c * P:(c + 1) * P],
                                     s_pe_work if t == blocks - 1 else None)
                marks[(key + "_read_src",)] = made

                def out_(i=i, bank=bank, c=c, made=made):
                    a, d = split_out(i, bank, P, dst_hi[:, c, :], dst_lo[:, c, :], made, free)
                    marks[(key, c)] = [a, d]
                defer(out_)
                yield

        def project(b_key, hf, u):
            for name, col in (("q", hf * P), ("k", dim + hf * P)):
                i, bank = work_bank()
                pe.wait(*got(("xt", 0), ("xt", 1)), wqkv_done)
                terms = [(w, xx) for w, xx in ((wqkv_hi, xt_hi), (wqkv_hi, xt_lo), (wqkv_lo, xt_hi))]
                n = 0
                for w, xx in terms:
                    for c in range(kd):
                        made = mm(bank[:, :], w[:, c, col:col + P], xx[:, c, :], n == 0, n == 5,
                                  s_pe_work if n == 5 else None)
                        n += 1
                marks[("xt_read",)] = made

                def out_(i=i, bank=bank, name=name, made=made):
                    marks[("staged", name)] = list(split_out(i, bank, P, staged[name + "_hi"][:, :],
                                                             staged[name + "_lo"][:, :], made, maybe(("staged_read", u - 1))))
                defer(out_)
                yield

        def values(b):
            for t0 in range(0, blocks, 2):
                i, bank = work_bank()
                pe.wait(*got(("xt", 0), ("xt", 1)), wqkv_done)
                for t in range(2):
                    n = 0
                    for w, xx in ((wqkv_hi, xt_hi), (wqkv_lo, xt_hi), (wqkv_hi, xt_lo)):
                        for c in range(kd):
                            made = mm(bank[:, t * dim:(t + 1) * dim], xx[:, c, (t0 + t) * P:(t0 + t + 1) * P],
                                      w[:, c, 2 * dim:3 * dim], n == 0, n == 5, s_pe_work if (t, n) == (1, 5) else None)
                            n += 1
                marks[("xt_read",)] = made

                def out_(i=i, bank=bank, t0=t0, made=made):
                    act.wait(made, v_ones_done, *maybe(("pv_done", 2 * b - 3)))
                    done = act.put(lambda e: e.activation(v_ones[b % 2][:, t0:t0 + 2, :, 0:HEAD_DIM],
                                                          bank[:, :].rearrange("p (t h d) -> p t h d", t=2, d=HEAD_DIM),
                                                          ACT.Copy), s_act)
                    work_free[i] = [done]
                    marks[("v", b, t0)] = done
                defer(out_)
                yield

        def spread(u):
            z = u % 2
            names = ("q_hi", "q_lo", "k_hi", "k_lo")
            sp.wait(edges_done, *got(("staged", "q"), ("staged", "k")), *maybe(("spread", u - 2)))
            for n, name in enumerate(names):
                last = sp.put(lambda e, n=n, name=name: e.dma_start(
                    bounce[z, n].rearrange("d h t -> h d t"), staged[name][:, :].bitcast(F32)), s_bounced[z], 16)
            marks[("staged_read", u)] = last
            sp.wait(last, *maybe(("scores2", u - 2)))
            for rows, r0, n0, n in ((q_rows[z], 0, 0, 2), (q_rows[z], 2, 0, 2), (k_rows[z], 0, 2, 2),
                                    (k_rows[z], 2, 3, 1), (k_rows[z], 3, 2, 1)):
                last = sp.put(lambda e, rows=rows, r0=r0, n0=n0, n=n: e.dma_start(
                    rows[r0 * HEAD_DIM:(r0 + n) * HEAD_DIM, :, :].bitcast(F32),
                    bounce[z, n0:n0 + n].rearrange("n d h t -> (n d) h t")), s_spread[z], 16)
            marks[("spread", u)] = last

        def scores_max(u):
            q, k, m = q_rows[u % 2], k_rows[u % 2], row_max[u % 2]
            for h0 in range(0, UNIT_HEADS, GROUP):
                for qb in range(blocks):
                    n = (qb + 1) * P
                    heads = BANK // n
                    for h in range(h0, h0 + GROUP, heads):
                        i, bank = work_bank()
                        pe.wait(*got(("spread", u)), ident_done)
                        for g in range(heads):
                            mm(bank[:, g * n:(g + 1) * n], q[0:ROWS1, h + g, qb * P:(qb + 1) * P],
                               k[0:ROWS1, h + g, 0:n], True, False)
                            made = mm(bank[:, g * n + n - P:(g + 1) * n], ident_bf[:, :], mask_bf[:, :], False, True,
                                      s_pe_work if g == heads - 1 else None)

                        def out_(i=i, bank=bank, h=h, n=n, heads=heads, qb=qb, made=made):
                            dve.wait(made, *maybe(("max_read", u - 2)))
                            done = dve.put(lambda e: e.tensor_reduce(
                                m[:, qb, h:h + heads], bank[:, 0:heads * n].rearrange("p (h n) -> p h n", n=n),
                                AX.X, ALU.max), s_dve_max)
                            work_free[i] = [done]
                            marks[("max", u)] = done
                        defer(out_)
                        yield

        def max_rows(u):
            flush()
            i, bank = work_bank()
            pe.wait(*got(("max", u)))
            for qb in range(blocks):
                made = transpose(bank[0:UNIT_HEADS, qb * P:(qb + 1) * P], row_max[u % 2][:, qb, :],
                                 s_pe_work if qb == blocks - 1 else None)
            marks[("max_read", u)] = made
            a, d = split_out(i, bank, UNIT_HEADS, max_hi[:, :], max_lo[:, :], made, maybe(("maxrow", u - 1)))
            sp.wait(a, d, *maybe(("scores2", u - 2)))
            for r, src in enumerate((max_hi, max_lo)):
                last = sp.put(lambda e, r=r, src=src: e.dma_start(
                    q_rows[u % 2][ROWS1 + r:ROWS1 + r + 1, :, :].bitcast(F32), src[:, :].bitcast(F32)),
                    s_maxrow[u % 2], 16)
            marks[("maxrow", u)] = last
            yield

        score_free, score_next = [[], [], []], [0]
        probs_free, probs_next = [[edges_done] for _ in range(3)], [0]

        def attend(u):
            b, hf = u // 2, u % 2
            q, k, v = q_rows[hf], k_rows[hf], v_ones[b % 2]
            late = []

            def step():
                for x_ in late:
                    x_[0] -= 1
                while late and late[0][0] <= 0:
                    late.pop(0)[1]()

            for g in range(UNIT_HEADS // GROUP):
                for j in range(blocks):
                    n = tokens - j * P
                    heads = BANK // n if n <= 256 else 1
                    slot = probs_next[0] % 3
                    probs_next[0] += 1
                    state = {"exps": None}
                    free = list(probs_free[slot])
                    for h in range(0, GROUP, heads):
                        i = score_next[0] % 3
                        score_next[0] += 1
                        bank = score_banks[i]
                        assert score_free[i] is not None
                        pe.wait(*score_free[i], *got(("maxrow", u)))
                        score_free[i] = None
                        for e_ in range(heads):
                            hh = g * GROUP + h + e_
                            mm(bank[:, e_ * n:(e_ + 1) * n], k[0:ROWS2, hh, j * P:(j + 1) * P],
                               q[0:ROWS2, hh, j * P:tokens], True, False)
                            made = mm(bank[:, e_ * n:e_ * n + P], mask_bf[:, :], ident_bf[:, :], False, True,
                                      s_pe_score if e_ == heads - 1 else None)
                        marks[("scores2", u)] = made

                        def exp_(i=i, bank=bank, h=h, n=n, heads=heads, slot=slot, made=made, free=free, state=state):
                            act.wait(made, *free)
                            done = act.put(lambda e: e.activation(
                                probs[slot][:, h:h + heads, 0:n], bank[:, 0:heads * n].rearrange("p (h n) -> p h n", n=n),
                                ACT.Exp, scale=scale), s_act_exp)
                            score_free[i] = [done]
                            state["exps"] = done
                        late.append([1, exp_])
                        step()
                        yield

                    def pv_(g=g, j=j, n=n, slot=slot, state=state):
                        pe.wait(state["exps"], *got(("v", b, (j // 2) * 2)), v_ones_done)
                        if j == 0:
                            pe.wait(*maybe(("pv_bank_free",)))
                        for h in range(GROUP):
                            done = mm(pv_bank[32 * h:32 * h + 32, j * P:tokens], v[:, j, hf * UNIT_HEADS + g * GROUP + h, :],
                                      probs[slot][:, h, 0:n], j == 0, j == blocks - 1,
                                      s_pe_pv if h == GROUP - 1 else None, tile_position=(0, 32 * h))
                        probs_free[slot] = [done]
                        marks[("pv_done", u)] = done
                    late.append([3, pv_])

                def normalise(g=g):
                    z = g % 2
                    act.wait(*got(("pv_done", u)), *maybe(("pv_t_read", z)))
                    copied = act.put(lambda e: e.activation(pv_t[z][:, :], pv_bank[:, :], ACT.Copy), s_act)
                    marks[("pv_bank_free",)] = copied
                    flush()
                    i, bank = work_bank()
                    pe.wait(copied)
                    for t in range(blocks):
                        made = transpose(bank[:, t * P:(t + 1) * P], pv_t[z][:, t * P:(t + 1) * P],
                                         s_pe_work if t == blocks - 1 else None)
                    marks[("pv_t_read", z)] = made
                    both = bank[:, :].rearrange("p (t h c) -> p t h c", t=blocks, c=2 * HEAD_DIM)
                    dve.wait(made, *maybe(("rden_read", z)))
                    inverse = dve.put(lambda e: e.reciprocal(rden[z][:, :, :], both[:, :, :, HEAD_DIM]), s_dve)
                    dve.wait(inverse, *maybe(("attn_read",)))
                    c0 = (hf * UNIT_HEADS + g * GROUP) * HEAD_DIM
                    r = rden[z][:, :, :]
                    wide = bass.AP(tensor=r.tensor, offset=r.offset, ap=[list(a) for a in r.ap] + [[0, HEAD_DIM]])
                    o = attn[:, :, c0:c0 + GROUP * HEAD_DIM].rearrange("p t (h d) -> p t h d", d=HEAD_DIM)
                    last = None
                    for t in range(blocks):
                        last = dve.put(lambda e, t=t: e.tensor_tensor(o[:, t], both[:, t, :, 0:HEAD_DIM], wide[:, t], ALU.mult), s_dve)
                    marks[("rden_read", z)] = last
                    work_free[i] = [inverse, last]
                    marks[("attn", b)] = last
                late.append([3, normalise])
            while late:
                step()
                yield

        def project_out(b):
            for t0 in range(0, blocks, 2):
                i, bank = work_bank()
                pe.wait(*got(("attn_t", 0), ("attn_t", 1)), wqkv_done)
                for t in range(2):
                    n = 0
                    for w, a in ((wout_hi, wide_hi), (wout_lo, wide_hi), (wout_hi, wide_lo)):
                        for c in range(kd):
                            made = mm(bank[:, t * dim:(t + 1) * dim], a[:, c, (t0 + t) * P:(t0 + t + 1) * P],
                                      w[:, c, :], n == 0, n == 5, s_pe_work if (t, n) == (1, 5) else None)
                            n += 1
                marks[("attn_t_read",)] = made

                def out_(i=i, bank=bank, t0=t0, made=made):
                    dve.wait(made, x_in[b], *maybe(("x1_read", b - 2)))
                    added = dve.put(lambda e: e.tensor_tensor(
                        x1[b % 2][:, t0:t0 + 2, :], bank[:, :].rearrange("p (t d) -> p t d", t=2),
                        x_sb[b % 3][:, t0:t0 + 2, :], ALU.add), s_dve)
                    work_free[i] = [added]
                    marks[("x_read", b)] = added
                    dve.wait(added)
                    for t in range(t0, t0 + 2):
                        stat = dve.put(lambda e, t=t: e.bn_stats(stats1[:, t, :], x1[b % 2][:, t, :]), s_dve)
                    dve.wait(stat)
                    for t in range(t0, t0 + 2):
                        agg = dve.put(lambda e, t=t: e.bn_aggr(moments1[:, t, :], stats1[:, t, :]), s_dve)
                    marks[("moments1",)] = agg
                defer(out_)
                yield
            flush()
            dve.wait(*got(("moments1",)))
            vdone = dve.put(lambda e: e.tensor_scalar(var1[:, :], moments1[:, :, 1], EPS, None, ALU.add), s_dve)
            pool.wait(vdone)
            rdone = pool.put(lambda e: e.tensor_tensor(rstd1[:, :], var1[:, :], minus_half[:, :], ALU.pow), s_pool)
            yield
            dve.wait(rdone)
            for t in range(blocks):
                done = dve.put(lambda e, t=t: e.tensor_scalar(x1[b % 2][:, t, :], x1[b % 2][:, t, :], moments1[:, t, 0:1],
                                                              rstd1[:, t:t + 1], ALU.subtract, ALU.mult), s_dve)
            marks[("x1", b)] = x1_done[b] = done
            yield

        def ffn(b, part):
            t0 = part * 2
            cols = slice(part * half_tokens, (part + 1) * half_tokens)
            made_h = {}

            def down(m):
                pe.wait(*made_h[m], ffn_weights_done)
                if m == 0:
                    pe.wait(*maybe(("down_free",)))
                for n, hh in enumerate((h_hi[m % 2], h_lo[m % 2])):
                    for t in range(2):
                        done = mm(down_bank[:, t, :], hh[:, t * P:(t + 1) * P], wdown_t[:, m, :],
                                  (m, n, t) == (0, 0, 0), m == kh - 1, s_pe_down if (n, t) == (1, 1) else None)
                marks[("down", m % 2)] = done

            for m in range(kh):
                i, bank = work_bank()
                pe.wait(*got(("x1t", 0), ("x1t", 1)), ffn_weights_done)
                for g, w in enumerate((wgate_t, wup_t)):
                    n = 0
                    for xx in (wide_hi, wide_lo):
                        for c in range(kd):
                            made = mm(bank[:, g * half_tokens:(g + 1) * half_tokens], w[:, c, m * P:(m + 1) * P],
                                      xx[:, c, cols], n == 0, n == 3, s_pe_work if (g, n) == (1, 3) else None)
                            n += 1
                marks[("x1t_read",)] = made

                def out_(i=i, bank=bank, m=m, made=made):
                    z = m % 2
                    gate, up = bank[:, 0:half_tokens], bank[:, half_tokens:2 * half_tokens]
                    act.wait(made, *maybe(("h_split", z)))
                    t_done = act.put(lambda e: e.activation(h_full[z][:, :], gate, ACT.Tanh, scale=0.5 * W_SCALE), s_act)
                    dve.wait(made, t_done)
                    s_done = dve.put(lambda e: e.scalar_tensor_tensor(h_full[z][:, :], h_full[z][:, :], 1.0, gate,
                                                                      ALU.add, ALU.mult), s_dve)
                    marks[("silu_made", z)] = s_done
                    dve.wait(s_done)
                    h_done = dve.put(lambda e: e.scalar_tensor_tensor(h_full[z][:, :], h_full[z][:, :], 0.5 * W_SCALE * W_SCALE,
                                                                      up, ALU.mult, ALU.mult), s_dve)
                    marks[("h_made", z)] = h_done
                    work_free[i] = [t_done, s_done, h_done]
                    act.wait(h_done, *maybe(("down", z)))
                    hi_done = act.put(lambda e: e.activation(h_hi[z][:, :], h_full[z][:, :], ACT.Copy), s_act)
                    pool.wait(hi_done, *maybe(("down", z)))
                    lo_done = pool.put(lambda e: e.tensor_tensor(h_lo[z][:, :], h_full[z][:, :],
                                                                 h_hi[z][:, :].bitcast(F32), ALU.subtract), s_pool)
                    marks[("h_split", z)] = [hi_done, lo_done]
                    made_h[m] = [hi_done, lo_done]
                defer(out_)
                if m >= 2:
                    down(m - 2)
                yield
            flush()
            down(kh - 2)
            yield
            down(kh - 1)
            z = part
            down_done = marks[("down", (kh - 1) % 2)]
            dve.wait(down_done, x1_done[b], *maybe(("stored", z)))
            added = dve.put(lambda e: e.scalar_tensor_tensor(result[z][:, :, :], down_bank[:, :, :], W_SCALE,
                                                             x1[b % 2][:, t0:t0 + 2, :], ALU.mult, ALU.add), s_dve)
            marks[("down_free",)] = added
            marks[("x1_read", b)] = added
            dve.wait(added)
            for t in range(2):
                stat = dve.put(lambda e, t=t: e.bn_stats(stats2[:, t, :], result[z][:, t, :]), s_dve)
            dve.wait(stat)
            for t in range(2):
                agg = dve.put(lambda e, t=t: e.bn_aggr(moments2[:, t, :], stats2[:, t, :]), s_dve)
            dve.wait(agg)
            vdone = dve.put(lambda e: e.tensor_scalar(var2[:, :], moments2[:, :, 1], EPS, None, ALU.add), s_dve)
            pool.wait(vdone)
            rdone = pool.put(lambda e: e.tensor_tensor(rstd2[:, :], var2[:, :], minus_half[:, 0:2], ALU.pow), s_pool)
            yield
            yield
            dve.wait(rdone)
            for t in range(2):
                done = dve.put(lambda e, t=t: e.tensor_scalar(result[z][:, t, :], result[z][:, t, :], moments2[:, t, 0:1],
                                                              rstd2[:, t:t + 1], ALU.subtract, ALU.mult), s_dve)
            sp.wait(done)
            marks[("stored", z)] = sp.put(lambda e: e.dma_start(
                out[b, t0 * P:(t0 + 2) * P, :].rearrange("(t p) d -> p t d", p=P), result[z][:, :, :]), s_store[z], 16)
            yield

        def others(w):
            if 0 <= w < units:
                spread(w)
            fb = (w - 4) // 2
            if 0 <= fb < batches:
                yield from ffn(fb, w % 2)
            if w % 2 == 1 and 0 <= (w - 3) // 2 < batches:
                b = (w - 3) // 2
                yield from transposed(attn, wide_hi, wide_lo, got(("attn", b)), maybe(("x1t_read",)), "attn_t")
                marks[("attn_read",)] = marks[("attn_t_read_src",)]
                flush()
                yield from project_out(b)
                if b + 3 < batches:
                    x_in[b + 3] = load_x(b + 3, *got(("x_read", b)))
                yield from transposed(x1[b % 2], wide_hi, wide_lo, got(("x1", b)), got(("attn_t_read",)), "x1t")
                flush()
            if 0 <= w < units:
                yield from scores_max(w)
            if w % 2 == 1 and (w + 1) // 2 < batches:
                b = (w + 1) // 2
                yield from transposed(x_sb[b % 3], xt_hi, xt_lo, [x_in[b]], maybe(("xt_read",)) + [edges_done], "xt")
                flush()
                yield from values(b)
            if 0 <= w + 1 < units:
                yield from project(None, (w + 1) % 2, w + 1)
            if 0 <= w < units:
                yield from max_rows(w)
            flush()

        if batches > 2:
            x_in[2] = load_x(2)
        for w in range(-1, units + 5):
            fill = list_of = others(w)
            main = attend(w - 1) if 0 <= w - 1 < units else iter(())
            LEAD, RATIO = 8, 2
            for _ in range(LEAD):
                next(fill, None)
            alive = True
            while alive:
                alive = next(main, "end") != "end"
                for _ in range(RATIO):
                    next(fill, None)
            for _ in fill:
                pass

        for z in range(2):
            sp.wait(marks[("stored", z)])

        block = ctx.enter_context(nc.Block())

        @block.sync
        def _(e):
            sp.play(e)

        @block.tensor
        def _(e):
            pe.play(e)

        @block.scalar
        def _(e):
            act.play(e)

        @block.vector
        def _(e):
            dve.play(e)

        @block.gpsimd
        def _(e):
            pool.play(e)


_INS = ["L0_attn_x", "L0_attn_Wqkv", "L0_attn_Wout", "L0_ffn_w_gate", "L0_ffn_w_up", "L0_ffn_w_down"]


def kernel(**inputs):
    import concourse.bacc as _bacc
    from concourse.bass_utils import run_bass_kernel_spmd as _run

    nc = _bacc.Bacc("TRN2", target_bir_lowering=False, num_devices=1)
    arrays, args = {}, []
    tables = constants(inputs["L0_attn_x"].shape[1], HEAD_DIM ** -0.5)
    named = [(n, np.ascontiguousarray(inputs[n])) for n in _INS] + list(zip(("edge_rows", "squares"), tables))
    for name, a in named:
        arrays[name] = a
        args.append(nc.dram_tensor(name, a.shape, mybir.dt.from_np(a.dtype), kind="ExternalInput").ap())
    out = nc.dram_tensor("out", inputs["L0_attn_x"].shape, F32, kind="ExternalOutput").ap()
    build(nc, *args, out)
    return _run(nc, [arrays], core_ids=[0]).results[0]["out"]
```

```python
from contextlib import ExitStack

import numpy as np

import concourse.bass as bass
from concourse import mybir

F32 = mybir.dt.float32
F32R = mybir.dt.float32r
BF16 = mybir.dt.bfloat16
I32 = mybir.dt.int32
ALU = mybir.AluOpType
ACT = mybir.ActivationFunctionType
AX = mybir.AxisListType

P = 128
HEADS, HEAD_DIM = 16, 16
UNIT_HEADS = P // HEAD_DIM
GROUP = 4
SPLIT_ROWS = 4 * HEAD_DIM
ALIBI_ROWS = 4
MAX_ROWS = 2
PASS1_ROWS = 96
MAX_ROW = PASS1_ROWS
MIN_COLUMNS = 256
BANK = 512
COARSE_ROW = MAX_ROW + MAX_ROWS

OTHERS_COST, ATTEND_COST, FIRST_PASS_COST = (13.0, 18.0), 13.0, 9.5
CHAIN = 2.5
SELECT_LAG = 1
PV_LAG = 9
DIVIDE_LAG = 7
POW_LAG = 8
MAX_BANKS, SCORE_BANKS = 3, 2
PROBS_BUFFERS = 3
MASKED = -3.0e38
COARSELY_MASKED = -2.0 ** 100
EPS = 1e-5
W_SCALE = float(np.float32(1.0 / 127.0))


class Sem:

    def __init__(self, handle):
        self.handle, self.count = handle, 0


class Queue:

    def __init__(self):
        self.steps, self.reached = [], {}

    def wait(self, *marks):
        for sem, value in marks:
            if self.reached.get(sem, 0) < value:
                self.reached[sem] = value
                self.steps.append(lambda e, s=sem.handle, v=value: e.wait_ge(s, v))

    def put(self, instruction, sem=None, by=1):
        if sem is None:
            self.steps.append(instruction)
            return None
        self.steps.append(lambda e, f=instruction, s=sem.handle, n=by: f(e).then_inc(s, n))
        sem.count += by
        return (sem, sem.count)

    def play(self, engine):
        for step in self.steps:
            step(engine)


def alibi_slopes():
    start = 2.0 ** (-(8.0 / HEADS))
    return np.asarray([start * start ** i for i in range(HEADS)], dtype=np.float32)


def constants(tokens, scale):
    slopes = alibi_slopes() / np.float32(scale)
    slope_hi = (slopes.view(np.uint32) & np.uint32(0xFFFFF000)).view(np.float32)
    slope_lo = slopes - slope_hi
    position = np.arange(tokens, dtype=np.float32) - tokens // 2
    ones = np.ones(tokens, np.float32)
    coarse = P - COARSE_ROW
    rows = np.zeros((ALIBI_ROWS + MAX_ROWS + coarse, 2, HEADS, tokens), np.float32)
    stretch = np.arange(tokens) // -(-tokens // coarse)
    for h in range(HEADS):
        rows[0, 0, h], rows[0, 1, h] = slope_hi[h] * ones, position
        rows[1, 0, h], rows[1, 1, h] = slope_lo[h] * ones, position
        rows[2, 0, h], rows[2, 1, h] = position, -slope_hi[h] * ones
        rows[3, 0, h], rows[3, 1, h] = position, -slope_lo[h] * ones
        rows[4, 1, h] = rows[5, 1, h] = -ones
        for s in range(coarse):
            rows[6 + s, 0, h] = stretch == s
            rows[6 + s, 1, h] = np.where(stretch > s, np.float32(COARSELY_MASKED), np.float32(0))
    identity = np.eye(P, dtype=np.float32)
    mask = np.where(np.arange(P)[None, :] > np.arange(P)[:, None], np.float32(MASKED), np.float32(0))
    return rows, np.stack([identity, mask.astype(np.float32)], 1)


def build(nc, x, w_qkv, w_out, w_gate, w_up, w_down, edge_rows, squares, out):
    batches, tokens, dim = x.shape
    hidden = w_gate.shape[0]
    blocks = tokens // P
    kd = dim // P
    kh = hidden // P
    scale = HEAD_DIM ** -0.5
    units = batches * 2
    half_tokens = tokens // 2
    assert tokens == BANK and HEADS == 2 * UNIT_HEADS and kd == 2 and blocks == 4

    with ExitStack() as ctx:
        def sb(name, shape, dt=F32):
            return ctx.enter_context(nc.sbuf_tensor(name, shape, dt))

        def ps(name, shape, dt=F32):
            return ctx.enter_context(nc.psum_tensor(name, shape, dt))

        def sem(name):
            return Sem(ctx.enter_context(nc.semaphore(name)))

        wqkv_hi, wqkv_lo = sb("wqkv_hi", [P, kd, 3 * dim], F32R), sb("wqkv_lo", [P, kd, 3 * dim], F32R)
        wout_hi, wout_lo = sb("wout_hi", [P, kd, dim], F32R), sb("wout_lo", [P, kd, dim], F32R)
        wgate_t, wup_t = sb("wgate_t", [P, kd, hidden], F32R), sb("wup_t", [P, kd, hidden], F32R)
        wdown_t = sb("wdown_t", [P, kh, dim], F32R)
        ident = sb("ident", [P, P])
        ident_bf, mask_bf = sb("ident_bf", [P, P], BF16), sb("mask_bf", [P, P], BF16)
        minus_half = sb("minus_half", [P, blocks])
        q_rows = [sb(f"q_rows{i}", [P, UNIT_HEADS, tokens], F32R) for i in range(2)]
        k_rows = [sb(f"k_rows{i}", [P, UNIT_HEADS, tokens], F32R) for i in range(2)]
        staged_hi, staged_lo = sb("staged_hi", [P, 2, tokens], F32R), sb("staged_lo", [P, 2, tokens], F32R)
        v_ones = [sb(f"v_ones{i}", [P, blocks, HEADS, 2 * HEAD_DIM]) for i in range(2)]
        x_sb = sb("x_sb", [P, blocks, dim])
        xt_hi, xt_lo = sb("xt_hi", [P, kd, tokens], F32R), sb("xt_lo", [P, kd, tokens], F32R)
        probs = [sb(f"probs{i}", [P, GROUP, tokens]) for i in range(PROBS_BUFFERS)]
        row_max = [sb(f"row_max{i}", [P, blocks, UNIT_HEADS]) for i in range(2)]
        max_hi, max_lo = sb("max_hi", [GROUP, tokens], F32R), sb("max_lo", [GROUP, tokens], F32R)
        pv_t = [sb(f"pv_t{i}", [P, tokens]) for i in range(2)]
        rden = [sb(f"rden{i}", [P, blocks, GROUP]) for i in range(2)]
        attn = sb("attn", [P, blocks, dim])
        x1 = [sb(f"x1_{i}", [P, blocks, dim]) for i in range(2)]
        x1t_hi, x1t_lo = sb("x1t_hi", [P, kd, tokens], F32R), sb("x1t_lo", [P, kd, tokens], F32R)
        stats1, moments1 = sb("stats1", [P, blocks, 6]), sb("moments1", [P, blocks, 2])
        stats2, moments2 = sb("stats2", [P, 2, 6]), sb("moments2", [P, 2, 2])
        var1, rstd1 = sb("var1", [P, blocks]), sb("rstd1", [P, blocks])
        var2, rstd2 = sb("var2", [P, 2]), sb("rstd2", [P, 2])
        h_full = [sb(f"h_full{i}", [P, half_tokens]) for i in range(2)]
        h_hi, h_lo = sb("h_hi", [P, kh, half_tokens], F32R), sb("h_lo", [P, kh, half_tokens], F32R)
        result = [sb(f"result{i}", [P, 2, dim]) for i in range(2)]

        bounce = nc.dram_tensor("bounce", [2, 4, HEAD_DIM, UNIT_HEADS, tokens], F32, kind="Internal").ap()

        edge_copy = nc.dram_tensor("edge_copy", list(edge_rows.shape), F32, kind="Internal").ap()

        score_banks = [ps(f"score_bank{i}", [P, BANK]) for i in range(SCORE_BANKS)]
        max_banks = [ps(f"max_bank{i}", [P, BANK]) for i in range(MAX_BANKS)]
        work_banks = [ps(f"work_bank{i}", [P, BANK]) for i in range(2)]
        pv_bank = ps("pv_bank", [P, BANK])

        pe, act, dve, pool, sp = Queue(), Queue(), Queue(), Queue(), Queue()

        s_const, s_weights = sem("s_const"), sem("s_weights")
        s_x, s_residual = sem("s_x"), [sem(f"s_residual{i}") for i in range(2)]
        s_spread = [[sem(f"s_spread{i}{g}") for g in range(2)] for i in range(2)]
        s_bounced = [sem(f"s_bounced{i}") for i in range(2)]
        s_edge = sem("s_edge")
        s_maxrow = [[sem(f"s_maxrow{i}{g}") for g in range(2)] for i in range(2)]
        s_store = [sem(f"s_store{i}") for i in range(2)]
        s_pe_work, s_pe_score, s_pe_pv = (sem(n) for n in ("s_pe_work", "s_pe_score", "s_pe_pv"))
        s_act, s_act_exp, s_dve, s_dve_max, s_pool = (sem(n) for n in ("s_act", "s_act_exp", "s_dve", "s_dve_max", "s_pool"))

        class Ring:
            def __init__(self, banks):
                self.banks, self.free, self.turn = banks, [[] for _ in banks], 0

            def take(self):
                i = self.turn % len(self.banks)
                self.turn += 1
                while self.free[i] is None:
                    pending.pop(0)[1]()
                pe.wait(*self.free[i])
                self.free[i] = None

                def release(*marks_):
                    self.free[i] = list(marks_)
                return release, self.banks[i]

        work, maxima, scores = Ring(work_banks), Ring(max_banks), Ring(score_banks)

        def mm(o, lhs, rhs, start, stop, sem=None, **kw):
            return pe.put(lambda e, o=o, l=lhs, r=rhs: e.matmul(o, l, r, start=start, stop=stop,
                                                                skip_group_check=True, **kw), sem)

        def transpose(o, i, sem=None):
            n = i.shape[0]
            return pe.put(lambda e: e.transpose(o, i, ident[0:n, 0:n]), sem)

        def split_out(release, bank, rows, hi, lo, made, free, then):
            src = bank[0:rows, :]
            act.wait(made, *free)
            hi_done = act.put(lambda e: e.activation(hi, src, ACT.Copy), s_act)

            def low():
                dve.wait(made, hi_done, *free)
                lo_done = dve.put(lambda e: e.tensor_tensor(lo, src, hi.bitcast(F32), ALU.subtract), s_dve)
                release(hi_done, lo_done)
                then(hi_done, lo_done)
            later(1, low)

        pending, clock = [], [0]

        def later(steps, f):
            pending.append((clock[0] + steps, f))
            pending.sort(key=lambda x: x[0])

        def tick():
            clock[0] += 1
            while pending and pending[0][0] <= clock[0]:
                pending.pop(0)[1]()

        def advance():
            pending.pop(0)[1]()

        def flush():
            while pending:
                advance()

        def flat(buffer, size):
            dims = " ".join("abc"[:len(buffer.shape) - 1])
            return buffer[:].rearrange(f"p {dims} -> p ({dims})")[:, 0:size]

        raw_qkv = flat(probs[0], kd * 3 * dim).rearrange("p (k n) -> p k n", k=kd)
        raw_out = flat(attn, kd * dim).rearrange("p (k n) -> p k n", k=kd)
        gate_f = flat(probs[1], kh * dim).rearrange("p (t n) -> p t n", t=kh)
        up_f = flat(probs[2], kh * dim).rearrange("p (t n) -> p t n", t=kh)
        down_f = flat(v_ones[1], kd * hidden).rearrange("p (t n) -> p t n", t=kd)
        squares_sb = x1[0][:, 0:1, :].rearrange("p a (s n) -> p (a s) n", s=2)

        def load_x(b, target, arrived, *free):
            sp.wait(*free)
            return sp.put(lambda e: e.dma_start(target[:, :, :], x[b].rearrange("(t p) d -> p t d", p=P)), arrived, 16)

        sp.put(lambda e: e.dma_start(squares_sb, squares), s_const, 16)
        const_in = (s_const, s_const.count)
        for rows in q_rows + k_rows:
            zeroed = pool.put(lambda e, rows=rows: e.memset(rows[SPLIT_ROWS:, :, :].bitcast(F32), 0.0), s_pool)
        edges_in = sp.put(lambda e: e.dma_start(edge_copy, edge_rows), s_edge, 16)
        x_in = {0: load_x(0, x_sb, s_x)}
        sp.put(lambda e: e.dma_start(raw_qkv, w_qkv.rearrange("(k p) n -> p k n", p=P)), s_weights, 16)
        sp.put(lambda e: e.dma_start(raw_out, w_out.rearrange("(k p) n -> p k n", p=P)), s_weights, 16)
        sp.put(lambda e: e.dma_start(gate_f.bitcast(I32), w_gate.rearrange("(t p) n -> p t n", p=P)), s_weights, 16)
        sp.put(lambda e: e.dma_start(up_f.bitcast(I32), w_up.rearrange("(t p) n -> p t n", p=P)), s_weights, 16)
        sp.put(lambda e: e.dma_start(down_f.bitcast(I32), w_down.rearrange("(t p) n -> p t n", p=P)), s_weights, 16)
        weights_in = (s_weights, s_weights.count)

        sp.wait(edges_in, zeroed)
        for z in range(2):
            heads = slice(z * UNIT_HEADS, (z + 1) * UNIT_HEADS)
            for rows, row, side, first, n in ((q_rows[z], SPLIT_ROWS, 0, 0, ALIBI_ROWS), (k_rows[z], SPLIT_ROWS, 1, 0, ALIBI_ROWS),
                                              (k_rows[z], MAX_ROW, 1, ALIBI_ROWS, P - MAX_ROW),
                                              (q_rows[z], COARSE_ROW, 0, ALIBI_ROWS + MAX_ROWS, P - COARSE_ROW)):
                edges_done = sp.put(lambda e, rows=rows, row=row, side=side, first=first, n=n, heads=heads: e.dma_start(
                    rows[row:row + n, :, :].bitcast(F32), edge_copy[first:first + n, side, heads, :]), s_edge, 16)

        dve.wait(const_in)
        dve.put(lambda e: e.tensor_copy(ident[:, :], squares_sb[:, 0, :]), s_dve)
        dve.put(lambda e: e.tensor_copy(ident_bf[:, :], squares_sb[:, 0, :]), s_dve)
        dve.put(lambda e: e.tensor_copy(mask_bf[:, :], squares_sb[:, 1, :]), s_dve)
        dve.put(lambda e: e.memset(minus_half[:, :], -0.5), s_dve)
        ident_done = dve.put(lambda e: e.memset(v_ones[0][:, :, :, HEAD_DIM:], 1.0), s_dve)
        dve.wait(weights_in)
        hi = dve.put(lambda e: e.tensor_copy(wqkv_hi[:, :, :], raw_qkv), s_dve)
        hi2 = dve.put(lambda e: e.tensor_copy(wout_hi[:, :, :], raw_out), s_dve)
        dve.put(lambda e: e.tensor_copy(gate_f, gate_f.bitcast(I32)), s_dve)
        dve.put(lambda e: e.tensor_copy(up_f, up_f.bitcast(I32)), s_dve)
        as_float = dve.put(lambda e: e.tensor_copy(down_f, down_f.bitcast(I32)), s_dve)
        dve.wait(hi, hi2)
        dve.put(lambda e: e.tensor_tensor(wqkv_lo[:, :, :], raw_qkv, wqkv_hi[:, :, :].bitcast(F32), ALU.subtract), s_dve)
        wqkv_done = dve.put(lambda e: e.tensor_tensor(wout_lo[:, :, :], raw_out, wout_hi[:, :, :].bitcast(F32), ALU.subtract), s_dve)
        dve.wait(as_float)
        residual_in = {}
        ffn_weights_done, v_ones_done = [], []
        marks = {}

        def got(*keys):
            return [m for k in keys for m in (marks[k] if isinstance(marks[k], list) else [marks[k]])]

        def maybe(*keys):
            return [m for k in keys if k in marks for m in (marks[k] if isinstance(marks[k], list) else [marks[k]])]

        def transposed(src, dst_hi, dst_lo, ready, free, key):
            for c in range(kd):
                release, bank = work.take()
                pe.wait(*ready)
                for t in range(blocks):
                    made = transpose(bank[:, t * P:(t + 1) * P], src[:, t, c * P:(c + 1) * P],
                                     s_pe_work if t == blocks - 1 else None)
                marks[(key + "_read_src",)] = made

                def out_(release=release, bank=bank, c=c, made=made):
                    split_out(release, bank, P, dst_hi[:, c, :], dst_lo[:, c, :], made, free,
                              lambda a, d: marks.update({(key, c): [a, d]}))
                later(1, out_)
                yield 0.45

        def project(hf, u):
            for side, col in enumerate((hf * P, dim + hf * P)):
                release, bank = work.take()
                pe.wait(*got(("xt", 0), ("xt", 1)), wqkv_done)
                terms = [(w, xx) for w, xx in ((wqkv_hi, xt_hi), (wqkv_hi, xt_lo), (wqkv_lo, xt_hi))]
                n = 0
                for w, xx in terms:
                    for c in range(kd):
                        made = mm(bank[:, :], w[:, c, col:col + P], xx[:, c, :], n == 0, n == 5,
                                  s_pe_work if n == 5 else None)
                        n += 1
                marks[("xt_read",)] = made

                def out_(release=release, bank=bank, side=side, made=made):
                    split_out(release, bank, P, staged_hi[:, side, :], staged_lo[:, side, :], made,
                              maybe(("staged_read", u - 1), ("attn_t_read",)), lambda a, d: marks.update({("staged", side): [a, d]}))
                later(1, out_)
                yield 1.3

        def values(b):
            for t0 in range(0, blocks, 2):
                release, bank = work.take()
                pe.wait(*got(("xt", 0), ("xt", 1)), wqkv_done)
                for t in range(2):
                    n = 0
                    for w, xx in ((wqkv_hi, xt_hi), (wqkv_lo, xt_hi), (wqkv_hi, xt_lo)):
                        for c in range(kd):
                            made = mm(bank[:, t * dim:(t + 1) * dim], xx[:, c, (t0 + t) * P:(t0 + t + 1) * P],
                                      w[:, c, 2 * dim:3 * dim], n == 0, n == 5, s_pe_work if (t, n) == (1, 5) else None)
                            n += 1
                marks[("xt_read",)] = made

                def out_(release=release, bank=bank, t0=t0, made=made):
                    act.wait(made, *maybe(("pv_done", 2 * b - 3)))
                    done = act.put(lambda e: e.activation(v_ones[b % 2][:, t0:t0 + 2, :, 0:HEAD_DIM],
                                                          bank[:, :].rearrange("p (t h d) -> p t h d", t=2, d=HEAD_DIM),
                                                          ACT.Copy), s_act)
                    release(done)
                    marks[("v", b, t0)] = done
                later(1, out_)
                yield 1.3

        def spread(u):
            z = u % 2
            parts = ((staged_hi, 0), (staged_lo, 0), (staged_hi, 1), (staged_lo, 1))
            sp.wait(*got(("staged", 0), ("staged", 1)), *maybe(("spread", u - 2, 0), ("spread", u - 2, 1)))
            for n, (source, side) in enumerate(parts):
                last = sp.put(lambda e, n=n, source=source, side=side: e.dma_start(
                    bounce[z, n].rearrange("d h t -> h d t"), source[:, side, :].bitcast(F32)), s_bounced[z], 16)
            marks[("staged_read", u)] = last

        def gather(u, g):
            z, heads = u % 2, slice(g * GROUP, (g + 1) * GROUP)
            sp.wait(edges_done, *got(("staged_read", u)), *maybe(("scores2", u - 2, g)))
            for rows, r0, n0, n in ((q_rows[z], 0, 0, 2), (q_rows[z], 2, 0, 2), (k_rows[z], 0, 2, 2),
                                    (k_rows[z], 2, 3, 1), (k_rows[z], 3, 2, 1)):
                last = sp.put(lambda e, rows=rows, r0=r0, n0=n0, n=n: e.dma_start(
                    rows[r0 * HEAD_DIM:(r0 + n) * HEAD_DIM, heads, :].bitcast(F32),
                    bounce[z, n0:n0 + n, :, heads, :].rearrange("n d h t -> (n d) h t")), s_spread[z][g], 16)
            marks[("spread", u, g)] = last

        def gather_first(u):
            if ("staged_read", u) in marks and (u < 2 or ("scores2_done", u - 2) in marks):
                gather(u, 0)

        def scores_max(u, g):
            q, k, m = q_rows[u % 2], k_rows[u % 2], row_max[u % 2]
            for qb in range(blocks):
                n = (qb + 1) * P
                width = max(n, MIN_COLUMNS)
                heads = BANK // width
                for h in range(g * GROUP, (g + 1) * GROUP, heads):
                    release, bank = maxima.take()
                    pe.wait(*got(("spread", u, g)), ident_done)
                    for a in range(heads):
                        c0 = a * width
                        mm(bank[:, c0:c0 + width], q[0:PASS1_ROWS, h + a, qb * P:(qb + 1) * P],
                           k[0:PASS1_ROWS, h + a, 0:width], True, False)
                        made = mm(bank[:, c0 + n - P:c0 + n], ident_bf[:, :], mask_bf[:, :], False, True,
                                  s_pe_work if a == heads - 1 else None)

                    def out_(release=release, bank=bank, h=h, n=n, width=width, heads=heads, qb=qb, made=made):
                        dve.wait(made, *maybe(("max_read", u - 2, g)))
                        done = dve.put(lambda e: e.tensor_reduce(
                            m[:, qb, h:h + heads], bank[:, 0:heads * width].rearrange("p (h n) -> p h n", n=width)[:, :, 0:n],
                            AX.X, ALU.max), s_dve_max)
                        release(done)
                        marks[("max", u, g)] = done
                        made_max[u, g] = made_max.get((u, g), 0) + 1
                    later(1, out_)
                    yield 0.13 * heads + 0.0004 * heads * width

        made_max = {}

        def max_rows(u, g):
            while made_max.get((u, g), 0) < 12:
                advance()
            release, bank = work.take()
            pe.wait(*got(("max", u, g)))
            heads = slice(g * GROUP, (g + 1) * GROUP)
            for qb in range(blocks):
                made = transpose(bank[0:GROUP, qb * P:(qb + 1) * P], row_max[u % 2][:, qb, heads],
                                 s_pe_work if qb == blocks - 1 else None)
            marks[("max_read", u, g)] = made

            def store(hi_done, lo_done):
                sp.wait(hi_done, lo_done, *maybe(("scores2", u - 2, g)))
                for r, src in enumerate((max_hi, max_lo)):
                    marks[("maxrow", u, g)] = marks[("maxrow",)] = sp.put(lambda e, r=r, src=src: e.dma_start(
                        q_rows[u % 2][MAX_ROW + r:MAX_ROW + r + 1, heads, :].bitcast(F32), src[:, :].bitcast(F32)),
                        s_maxrow[u % 2][g], 16)
            later(1, lambda: split_out(release, bank, GROUP, max_hi[:, :], max_lo[:, :], made, maybe(("maxrow",)), store))
            yield 0.4

        def first_pass(u):
            yield from scores_max(u, 0)
            second = scores_max(u, 1)
            for _ in range(3):
                yield next(second)
            yield from max_rows(u, 0)
            yield from second
            yield 0.0
            yield 0.0
            yield from max_rows(u, 1)

        probs_free, probs_next = [[wqkv_done], ffn_weights_done, ffn_weights_done], [0]

        def attend(u):
            b, hf = u // 2, u % 2
            q, k, v = q_rows[hf], k_rows[hf], v_ones[b % 2]
            for g in range(UNIT_HEADS // GROUP):
                for j in range(blocks):
                    n = tokens - j * P
                    width = max(n, MIN_COLUMNS)
                    skip = width - n
                    heads = BANK // width
                    slot = probs_next[0] % PROBS_BUFFERS
                    probs_next[0] += 1
                    state = {}
                    while probs_free[slot] is None:
                        advance()
                    free, probs_free[slot] = probs_free[slot], None
                    for h in range(0, GROUP, heads):
                        release, bank = scores.take()
                        while ("maxrow", u, g) not in marks:
                            advance()
                        pe.wait(*got(("maxrow", u, g)))
                        for e_ in range(heads):
                            hh = g * GROUP + h + e_
                            c0 = e_ * width
                            made = mm(bank[:, c0:c0 + width], k[:, hh, j * P:(j + 1) * P],
                                      q[:, hh, tokens - width:tokens], True, True, s_pe_score if e_ == heads - 1 else None)
                        marks[("scores2", u, g)] = made

                        def exp_(release=release, bank=bank, h=h, n=n, width=width, skip=skip, heads=heads, slot=slot, made=made, free=free, state=state):
                            act.wait(made, *free)
                            done = act.put(lambda e: e.activation(
                                probs[slot][:, h:h + heads, 0:n], bank[:, 0:heads * width].rearrange("p (h n) -> p h n", n=width)[:, :, skip:],
                                ACT.Exp, scale=scale), s_act_exp)
                            release(done)
                            state["exps"] = done
                        later(1, exp_)
                        if (g, j, h + heads) == (0, blocks - 1, GROUP):
                            marks[("scores2_done", u)] = made
                            gather_first(u + 2)
                        yield 0.2 + 0.0009 * n

                    def select_(slot=slot, state=state):
                        pool.wait(state["exps"])
                        diagonal = probs[slot][:, :, 0:P]
                        state["masked"] = pool.put(lambda e: e.affine_select(
                            out=diagonal, in_=diagonal, compare_op=ALU.is_ge, fill=0.0, base=0,
                            pattern=[[0, GROUP], [1, P]], channel_multiplier=-1), s_pool)
                    later(SELECT_LAG, select_)

                    def pv_(g=g, j=j, n=n, slot=slot, state=state):
                        pe.wait(state["exps"], state["masked"], *got(("v", b, (j // 2) * 2)), *v_ones_done)
                        if j == 0:
                            pe.wait(*maybe(("pv_bank_free",)))
                        for h in range(GROUP):
                            done = mm(pv_bank[32 * h:32 * h + 32, j * P:tokens], v[:, j, hf * UNIT_HEADS + g * GROUP + h, :],
                                      probs[slot][:, h, 0:n], j == 0, j == blocks - 1,
                                      s_pe_pv if h == GROUP - 1 else None, tile_position=(0, 32 * h))
                        probs_free[slot] = [done]
                        marks[("pv_done", u)] = done
                    later(PV_LAG, pv_)

                def normalise(g=g):
                    z = g % 2
                    act.wait(*got(("pv_done", u)), *maybe(("pv_t_read", z)))
                    copied = act.put(lambda e: e.activation(pv_t[z][:, :], pv_bank[:, :], ACT.Copy), s_act)
                    marks[("pv_bank_free",)] = copied
                    later(DIVIDE_LAG, lambda: divide(g, z, copied))

                def divide(g, z, copied):
                    release, bank = work.take()
                    pe.wait(copied)
                    for t in range(blocks):
                        made = transpose(bank[:, t * P:(t + 1) * P], pv_t[z][:, t * P:(t + 1) * P],
                                         s_pe_work if t == blocks - 1 else None)
                    marks[("pv_t_read", z)] = made
                    later(1, lambda: divide_out(g, z, release, bank, made))

                def divide_out(g, z, release, bank, made):
                    both = bank[:, :].rearrange("p (t h c) -> p t h c", t=blocks, c=2 * HEAD_DIM)
                    dve.wait(made, *maybe(("rden_read", z)))
                    inverse = dve.put(lambda e: e.reciprocal(rden[z][:, :, :], both[:, :, :, HEAD_DIM]), s_dve)
                    dve.wait(inverse, *maybe(("attn_read",)))
                    c0 = (hf * UNIT_HEADS + g * GROUP) * HEAD_DIM
                    r = rden[z][:, :, :]
                    wide = bass.AP(tensor=r.tensor, offset=r.offset, ap=[list(a) for a in r.ap] + [[0, HEAD_DIM]])
                    o = attn[:, :, c0:c0 + GROUP * HEAD_DIM].rearrange("p t (h d) -> p t h d", d=HEAD_DIM)
                    last = None
                    for t in range(blocks):
                        last = dve.put(lambda e, t=t: e.tensor_tensor(o[:, t], both[:, t, :, 0:HEAD_DIM], wide[:, t], ALU.mult), s_dve)
                    marks[("rden_read", z)] = last
                    release(inverse, last)
                    marks[("attn", b)] = last
                later(PV_LAG + 3, normalise)

        def project_out(b):
            for t0 in range(0, blocks, 2):
                release, bank = work.take()
                pe.wait(*got(("attn_t", 0), ("attn_t", 1)), wqkv_done)
                for t in range(2):
                    n = 0
                    for w, a in ((wout_hi, staged_hi), (wout_lo, staged_hi), (wout_hi, staged_lo)):
                        for c in range(kd):
                            made = mm(bank[:, t * dim:(t + 1) * dim], a[:, c, (t0 + t) * P:(t0 + t + 1) * P],
                                      w[:, c, :], n == 0, n == 5, s_pe_work if (t, n) == (1, 5) else None)
                            n += 1
                marks[("attn_t_read",)] = made

                def out_(release=release, bank=bank, t0=t0, made=made):
                    dve.wait(made, residual_in[b])
                    added = dve.put(lambda e: e.tensor_tensor(
                        x1[b % 2][:, t0:t0 + 2, :], bank[:, :].rearrange("p (t d) -> p t d", t=2),
                        x1[b % 2][:, t0:t0 + 2, :], ALU.add), s_dve)
                    release(added)
                    dve.wait(added)
                    for t in range(t0, t0 + 2):
                        stat = dve.put(lambda e, t=t: e.bn_stats(stats1[:, t, :], x1[b % 2][:, t, :]), s_dve)
                    dve.wait(stat)
                    for t in range(t0, t0 + 2):
                        agg = dve.put(lambda e, t=t: e.bn_aggr(moments1[:, t, :], stats1[:, t, :]), s_dve)
                    marks[("moments1",)] = agg
                later(1, out_)
                yield 1.3
            def variance():
                dve.wait(*got(("moments1",)))
                vdone = dve.put(lambda e: e.tensor_scalar(var1[:, :], moments1[:, :, 1], EPS, None, ALU.add), s_dve)
                pool.wait(vdone)
                rdone = pool.put(lambda e: e.tensor_tensor(rstd1[:, :], var1[:, :], minus_half[:, :], ALU.pow), s_pool)
                later(POW_LAG, lambda: normal(rdone))

            def normal(rdone):
                dve.wait(rdone)
                for t in range(blocks):
                    done = dve.put(lambda e, t=t: e.tensor_scalar(x1[b % 2][:, t, :], x1[b % 2][:, t, :], moments1[:, t, 0:1],
                                                                  rstd1[:, t:t + 1], ALU.subtract, ALU.mult), s_dve)
                marks[("x1", b)] = done
            later(2, variance)

        def ffn(b, part):
            t0 = part * 2
            cols = slice(part * half_tokens, (part + 1) * half_tokens)
            split = {}
            for m in range(kh):
                release, bank = work.take()
                pe.wait(*got(("x1t", 0), ("x1t", 1)), *ffn_weights_done)
                for g, w in enumerate((wgate_t, wup_t)):
                    n = 0
                    for xx in (x1t_hi, x1t_lo):
                        for c in range(kd):
                            made = mm(bank[:, g * half_tokens:(g + 1) * half_tokens], w[:, c, m * P:(m + 1) * P],
                                      xx[:, c, cols], n == 0, n == 3, s_pe_work if (g, n) == (1, 3) else None)
                            n += 1
                marks[("x1t_read",)] = made
                z = m % 2
                gate, up = bank[:, 0:half_tokens], bank[:, half_tokens:2 * half_tokens]

                def tanh_(z=z, gate=gate, made=made, m=m):
                    act.wait(made, *maybe(("h_split", z)))
                    marks[("tanh",)] = act.put(lambda e: e.activation(h_full[z][:, :], gate, ACT.Tanh, scale=0.5 * W_SCALE), s_act)

                def silu_(z=z, gate=gate, up=up, made=made, release=release):
                    dve.wait(made, marks[("tanh",)])
                    s_done = dve.put(lambda e: e.scalar_tensor_tensor(h_full[z][:, :], h_full[z][:, :], 1.0, gate,
                                                                      ALU.add, ALU.mult), s_dve)
                    dve.wait(s_done)
                    h_done = dve.put(lambda e: e.scalar_tensor_tensor(h_full[z][:, :], h_full[z][:, :], 0.5 * W_SCALE * W_SCALE,
                                                                      up, ALU.mult, ALU.mult), s_dve)
                    release(marks[("tanh",)], s_done, h_done)
                    marks[("h",)] = h_done

                def split_(z=z, m=m):
                    pool.wait(marks[("h",)], *maybe(("down_read",)))
                    hi_done = pool.put(lambda e: e.tensor_copy(h_hi[:, m, :], h_full[z][:, :]), s_pool)
                    pool.wait(hi_done)
                    lo_done = pool.put(lambda e: e.tensor_tensor(h_lo[:, m, :], h_full[z][:, :],
                                                                 h_hi[:, m, :].bitcast(F32), ALU.subtract), s_pool)
                    marks[("h_split", z)] = [lo_done]
                    split[m] = lo_done
                later(1, tanh_)
                later(2, silu_)
                later(3, split_)
                yield 0.9
            for _ in range(2):
                yield 0.0
            while kh - 1 not in split:
                advance()
            release, bank = work.take()
            for m in range(kh):
                pe.wait(split[m], *ffn_weights_done)
                for n, hh in enumerate((h_hi, h_lo)):
                    for t in range(2):
                        down_done = mm(bank[:, t * dim:(t + 1) * dim], hh[:, m, t * P:(t + 1) * P], wdown_t[:, m, :],
                                       (m, n, t) == (0, 0, 0), m == kh - 1,
                                       s_pe_work if (m, n, t) == (kh - 1, 1, 1) else None)
            marks[("down_read",)] = down_done
            yield 2.6
            z = part

            def residual():
                dve.wait(down_done, *got(("x1", b)), *maybe(("stored", z)))
                added = dve.put(lambda e: e.scalar_tensor_tensor(
                    result[z][:, :, :], bank[:, :].rearrange("p (t d) -> p t d", t=2), W_SCALE,
                    x1[b % 2][:, t0:t0 + 2, :], ALU.mult, ALU.add), s_dve)
                release(added)
                marks[("x1_read", b)] = added
                dve.wait(added)
                for t in range(2):
                    stat = dve.put(lambda e, t=t: e.bn_stats(stats2[:, t, :], result[z][:, t, :]), s_dve)
                dve.wait(stat)
                for t in range(2):
                    agg = dve.put(lambda e, t=t: e.bn_aggr(moments2[:, t, :], stats2[:, t, :]), s_dve)
                dve.wait(agg)
                vdone = dve.put(lambda e: e.tensor_scalar(var2[:, :], moments2[:, :, 1], EPS, None, ALU.add), s_dve)
                pool.wait(vdone)
                rdone = pool.put(lambda e: e.tensor_tensor(rstd2[:, :], var2[:, :], minus_half[:, 0:2], ALU.pow), s_pool)
                later(POW_LAG, lambda: normal(rdone))

            def normal(rdone):
                dve.wait(rdone)
                for t in range(2):
                    done = dve.put(lambda e, t=t: e.tensor_scalar(result[z][:, t, :], result[z][:, t, :], moments2[:, t, 0:1],
                                                                  rstd2[:, t:t + 1], ALU.subtract, ALU.mult), s_dve)
                sp.wait(done)
                marks[("stored", z)] = sp.put(lambda e: e.dma_start(
                    out[b, t0 * P:(t0 + 2) * P, :].rearrange("(t p) d -> p t d", p=P), result[z][:, :, :]), s_store[z], 16)
            later(1, residual)
            yield 0.0

        def others(w):
            b = (w - 3) // 2
            n = (w + 1) // 2
            if w % 2 == 1 and n < batches:
                yield from transposed(x_sb, xt_hi, xt_lo, [x_in[n], ident_done], maybe(("xt_read",)), "xt")
                if n + 1 < batches:
                    x_in[n + 1] = load_x(n + 1, x_sb, s_x, *got(("xt_read_src",)))
            if w % 2 == 1:
                yield CHAIN
                flush()
                if 0 <= b < batches:
                    yield from transposed(attn, staged_hi, staged_lo, got(("attn", b)), maybe(("staged_read", w)), "attn_t")
                    marks[("attn_read",)] = marks[("attn_t_read_src",)]
                    yield CHAIN
                    flush()
                    yield from project_out(b)
            elif n < batches:
                yield from values(n)
            if 0 <= w + 1 < units:
                yield from project((w + 1) % 2, w + 1)
                yield 0.0
                flush()
                spread(w + 1)
                gather_first(w + 1)
            if w % 2 == 0 and 0 <= (w - 2) // 2 < batches:
                m = (w - 2) // 2
                residual_in[m] = load_x(m, x1[m % 2], s_residual[m % 2], *maybe(("x1_read", m - 2)))
            if w == 0:
                yield from ffn_weights()
            part = (w - 4) // 2
            if 0 <= part < batches:
                yield from ffn(part, w % 2)
            if w % 2 == 1 and 0 <= b < batches:
                while ("x1", b) not in marks:
                    advance()
                marks.pop(("x1t", 1), None)
                yield from transposed(x1[b % 2], x1t_hi, x1t_lo, got(("x1", b)), maybe(("x1t_read",)), "x1t")
                yield 0.0
                while ("x1t", 1) not in marks:
                    advance()

        def ffn_weights():
            pe.wait(ident_done, as_float)
            for src, dst, tiles, parts in ((gate_f, wgate_t, kd, kh), (up_f, wup_t, kd, kh), (down_f, wdown_t, kh, kd)):
                for c in range(tiles):
                    for r0 in range(0, parts, 4):
                        n = min(4, parts - r0)
                        release, bank = work.take()
                        for r in range(n):
                            made = transpose(bank[:, r * P:(r + 1) * P], src[:, r0 + r, c * P:(c + 1) * P],
                                             s_pe_work if r == n - 1 else None)
                        act.wait(made)
                        done = act.put(lambda e, d=dst, c=c, r0=r0, n=n, bank=bank:
                                       e.activation(d[:, c, r0 * P:(r0 + n) * P], bank[:, 0:n * P], ACT.Copy), s_act)
                        release(done)
                        yield 0.45
            ffn_weights_done.append(done)
            dve.wait(done)
            v_ones_done.append(dve.put(lambda e: e.memset(v_ones[1][:, :, :, HEAD_DIM:], 1.0), s_dve))

        def window_threads(w):
            yield others(w), OTHERS_COST[w % 2]
            if 0 <= w - 1 < units:
                yield attend(w - 1), ATTEND_COST
            if 0 <= w < units:
                yield first_pass(w), FIRST_PASS_COST

        for w in range(-1, units + 5):
            if 0 <= w < units:
                gather(w, 1)
            threads = [[0.0, i, thread, cost] for i, (thread, cost) in enumerate(window_threads(w))]
            while threads:
                least = min(threads)
                cost = next(least[2], None)
                if cost is None:
                    threads.remove(least)
                else:
                    least[0] += cost / least[3]
                    tick()
        flush()

        for z in range(2):
            sp.wait(marks[("stored", z)])

        block = ctx.enter_context(nc.Block())

        @block.sync
        def _(e):
            sp.play(e)

        @block.tensor
        def _(e):
            pe.play(e)

        @block.scalar
        def _(e):
            act.play(e)

        @block.vector
        def _(e):
            dve.play(e)

        @block.gpsimd
        def _(e):
            pool.play(e)


_INS = ["L0_attn_x", "L0_attn_Wqkv", "L0_attn_Wout", "L0_ffn_w_gate", "L0_ffn_w_up", "L0_ffn_w_down"]


def kernel(**inputs):
    import concourse.bacc as _bacc
    from concourse.bass_utils import run_bass_kernel_spmd as _run

    nc = _bacc.Bacc("TRN2", target_bir_lowering=False, num_devices=1)
    arrays, args = {}, []
    tables = constants(inputs["L0_attn_x"].shape[1], HEAD_DIM ** -0.5)
    named = [(n, np.ascontiguousarray(inputs[n])) for n in _INS] + list(zip(("edge_rows", "squares"), tables))
    for name, a in named:
        arrays[name] = a
        args.append(nc.dram_tensor(name, a.shape, mybir.dt.from_np(a.dtype), kind="ExternalInput").ap())
    out = nc.dram_tensor("out", inputs["L0_attn_x"].shape, F32, kind="ExternalOutput").ap()
    build(nc, *args, out)
    return _run(nc, [arrays], core_ids=[0]).results[0]["out"]
```
